# Optimizing a Trainium2 kernel written in Bass

```python
import numpy as np
import jax
import jax.numpy as jnp

def _softmax(x, axis=-1):
    return jax.nn.softmax(x, axis=axis)

def _gelu(x):
    return jax.nn.gelu(x, approximate=True)

def _silu(x):
    return jax.nn.silu(x)

def _sigmoid(x):
    return jax.nn.sigmoid(x)

def _layernorm(x, axis=-1, eps=1e-05):
    m = jnp.mean(x, axis=axis, keepdims=True)
    v = jnp.var(x, axis=axis, keepdims=True)
    return (x - m) / jnp.sqrt(v + eps)

def _scatter_add(tgt, idx, src, axis=0):
    return tgt.at[idx].add(src)

def _segment_sum(src, seg, n):
    return jax.ops.segment_sum(src, seg, n)
kernel_name = 'mk_flamingo_gated_d1_seqx_r4_3b7e6b'

def setup_inputs(seed: int=0):
    np.random.seed(seed)
    _w = jnp.asarray

    def _rec_inputs():
        import jax
        import jax.numpy as jnp
        _rk = jax.random.key(seed)
        x = 7.22e-05 + 1 * jax.random.normal(jax.random.fold_in(_rk, 1), (32, 112, 256), jnp.float32)
        _lenS = 112 - jax.random.randint(jax.random.fold_in(_rk, 7), (32,), 0, max(1, 112 // 4) + 1, jnp.int32)
        _lenS2 = 375 - jax.random.randint(jax.random.fold_in(_rk, 8), (32,), 0, max(1, 375 // 4) + 1, jnp.int32)
        _ctx_1024P = jax.random.normal(jax.random.fold_in(_rk, 11), (32, 16, 256), jnp.float32)
        _ctx_1024c = jax.random.dirichlet(jax.random.fold_in(_rk, 511), 0.3 * jnp.ones((16,), jnp.float32), (32, 375))
        _ctx_1024t = jnp.einsum('bsk,bkd->bsd', _ctx_1024c, _ctx_1024P)
        _ctx_1024t = _ctx_1024t * jax.lax.rsqrt(jnp.mean(jnp.square(_ctx_1024t)) + 1e-12) * 0.953939
        ctx_1024 = 4.13588e-05 + 0.999923 * (_ctx_1024t + 0.3 * jax.random.normal(jax.random.fold_in(_rk, 611), (32, 375, 256), jnp.float32))
        _g = jax.random.normal(jax.random.fold_in(_rk, 9001), (2, 1), jnp.float32)
        _g = jnp.sign(_g) * jnp.maximum(jnp.abs(_g), 1.0) + (_g == 0) * 1.0
        g_xattn = _g[0]
        g_ffn = _g[1]
        return (x, ctx_1024, g_xattn, g_ffn)
    x, ctx_1024, g_xattn, g_ffn = _rec_inputs()

    def _L0_xattn_setup():
        import jax, jax.numpy as jnp
        import numpy as np
        EMB = 256
        HEADS = 16
        HEAD_DIM = EMB // HEADS
        key = jax.random.key(seed)
        ks = jax.random.split(key, 11)
        B, S = (4, 512)
        scale = 1.0 / np.sqrt(EMB)
        inp = {'query': jax.random.normal(ks[0], (B, S, EMB), jnp.float32), 'key': jax.random.normal(ks[1], (B, S, EMB), jnp.float32), 'value': jax.random.normal(ks[2], (B, S, EMB), jnp.float32), 'Wq': jax.random.normal(ks[3], (EMB, EMB), jnp.float32) * scale, 'bq': jnp.zeros((EMB,), jnp.float32), 'Wk': jax.random.normal(ks[4], (EMB, EMB), jnp.float32) * scale, 'bk': jnp.zeros((EMB,), jnp.float32), 'Wv': jax.random.normal(ks[5], (EMB, EMB), jnp.float32) * scale, 'bv': jnp.zeros((EMB,), jnp.float32), 'Wo': jax.random.normal(ks[6], (EMB, EMB), jnp.float32) * scale, 'bo': jnp.zeros((EMB,), jnp.float32)}
        return inp
    _L0_xattn_all = _L0_xattn_setup()
    _L0_xattn_in = {k: v for k, v in _L0_xattn_all.items() if k in ('Wq', 'bq', 'Wk', 'bk', 'Wv', 'bv', 'Wo', 'bo')}
    del _L0_xattn_all

    def _L0_ffn_setup():
        import jax, jax.numpy as jnp
        import numpy as np
        B, S, D = (4, 512, 256)
        E, K = (8, 2)
        H = 352
        key = jax.random.key(seed)
        kx, kr, k1, k2, k3 = jax.random.split(key, 5)
        s = 0.02
        return {'x': jax.random.normal(kx, (B, S, D), dtype=jnp.float32), 'w_router': jax.random.normal(kr, (E, D), dtype=jnp.float32) * s, 'w1': jax.random.normal(k1, (E, D, H), dtype=jnp.float32) * s, 'w2': jax.random.normal(k2, (E, H, D), dtype=jnp.float32) * s, 'w3': jax.random.normal(k3, (E, D, H), dtype=jnp.float32) * s}
    _L0_ffn_all = _L0_ffn_setup()
    _L0_ffn_in = {k: v for k, v in _L0_ffn_all.items() if k in ('w_router', 'w1', 'w2', 'w3')}
    del _L0_ffn_all
    return {'x': x, 'ctx_1024': ctx_1024, 'g_xattn': g_xattn, 'g_ffn': g_ffn, 'L0_xattn_Wq': _L0_xattn_in['Wq'], 'L0_xattn_bq': _L0_xattn_in['bq'], 'L0_xattn_Wk': _L0_xattn_in['Wk'], 'L0_xattn_bk': _L0_xattn_in['bk'], 'L0_xattn_Wv': _L0_xattn_in['Wv'], 'L0_xattn_bv': _L0_xattn_in['bv'], 'L0_xattn_Wo': _L0_xattn_in['Wo'], 'L0_xattn_bo': _L0_xattn_in['bo'], 'L0_ffn_w_router': _L0_ffn_in['w_router'], 'L0_ffn_w1': _L0_ffn_in['w1'], 'L0_ffn_w2': _L0_ffn_in['w2'], 'L0_ffn_w3': _L0_ffn_in['w3']}

def reference(x, ctx_1024, g_xattn, g_ffn, L0_xattn_Wq, L0_xattn_bq, L0_xattn_Wk, L0_xattn_bk, L0_xattn_Wv, L0_xattn_bv, L0_xattn_Wo, L0_xattn_bo, L0_ffn_w_router, L0_ffn_w1, L0_ffn_w2, L0_ffn_w3):
    import jax
    import jax.numpy as jnp

    def _L0_xattn_ref(query, key, value, Wq, bq, Wk, bk, Wv, bv, Wo, bo):
        import jax, jax.numpy as jnp
        import numpy as np
        EMB = 256
        HEADS = 16
        HEAD_DIM = EMB // HEADS
        B, S, E = query.shape
        H, D = (HEADS, HEAD_DIM)

        def split_heads(x):
            return x.reshape(B, -1, H, D).transpose(0, 2, 1, 3)
        Q = split_heads(query @ Wq + bq)
        K = split_heads(key @ Wk + bk)
        V = split_heads(value @ Wv + bv)
        scores = jnp.einsum('bhqd,bhkd->bhqk', Q, K) / jnp.sqrt(jnp.float32(D))
        attn = jax.nn.softmax(scores, axis=-1)
        out = jnp.einsum('bhqk,bhkd->bhqd', attn, V)
        out = out.transpose(0, 2, 1, 3).reshape(B, S, E)
        return out @ Wo + bo

    def _L0_ffn_ref(x, w_router, w1, w2, w3):
        import jax, jax.numpy as jnp
        import numpy as np
        B, S, D = (4, 512, 256)
        E, K = (8, 2)
        H = 352
        bsz, seqlen, dim = x.shape
        xf = x.reshape(-1, dim)
        scores = jax.nn.softmax(xf @ w_router.T, axis=-1)
        expert_weights, expert_indices = jax.lax.top_k(scores, K)
        h = jax.nn.silu(jnp.einsum('td,edh->eth', xf, w1)) * jnp.einsum('td,edh->eth', xf, w3)
        y = jnp.einsum('eth,ehd->etd', h, w2)
        y_t = jnp.swapaxes(y, 0, 1)
        sel = jnp.take_along_axis(y_t, expert_indices[:, :, None], axis=1)
        out = jnp.sum(expert_weights[:, :, None] * sel, axis=1)
        return out.reshape(bsz, seqlen, dim)
    x = x + jnp.tanh(g_xattn[0]) * _L0_xattn_ref(_layernorm(x, axis=-1), ctx_1024, ctx_1024, L0_xattn_Wq, L0_xattn_bq, L0_xattn_Wk, L0_xattn_bk, L0_xattn_Wv, L0_xattn_bv, L0_xattn_Wo, L0_xattn_bo)
    x = x + jnp.tanh(g_ffn[0]) * _L0_ffn_ref(_layernorm(x, axis=-1), L0_ffn_w_router, L0_ffn_w1, L0_ffn_w2, L0_ffn_w3)
    return x

_drawn_inputs = setup_inputs


def setup_inputs(seed=0):
    import zlib

    import numpy as np

    out = dict(_drawn_inputs(seed))
    spreads = {'L0_xattn_bq': (0.0, 0.488),
     'L0_xattn_bk': (0.0, 0.8),
     'L0_xattn_bv': (0.0, 0.1),
     'L0_xattn_bo': (0.0, 0.1)}
    factors = {'L0_ffn_w_router': 8.0, 'L0_ffn_w1': 8.0, 'L0_ffn_w2': 8.0, 'L0_ffn_w3': 8.0}
    for name, (base, spread) in spreads.items():
        noise = np.random.default_rng([zlib.crc32(name.encode()), seed]).standard_normal(out[name].shape)
        drawn = base * np.exp(spread * noise) if base else spread * noise
        out[name] = jnp.asarray(drawn.astype(out[name].dtype))
    for name, factor in factors.items():
        out[name] = (out[name] * factor).astype(out[name].dtype)
    return out
```

```python
import concourse.bass as bass
from concourse import mybir
from concourse.alu_op_type import AluOpType as ALU
from contextlib import ExitStack


def flamingo(nc, x, ctx_kv, g_xattn, g_ffn, Wq, bq, Wk, bk, Wv, bv, Wo, bo, w_router, w1, w2, w3, out):
    f32 = mybir.dt.float32
    B, SQ, EMB = x.shape
    with nc.sbuf_tensor("ident", [128, 128], f32) as ident, nc.sbuf_tensor("xa", [SQ, B, EMB], f32) as xa, \
            nc.sbuf_tensor("stats", [SQ, B, 6], f32) as stats:
        attention(nc, ident, xa, stats, x, ctx_kv, g_xattn, Wq, bq, Wk, bk, Wv, bv, Wo, bo)
        route_and_ffn(nc, ident, xa, stats, g_ffn, w_router, w1, w2, w3, out)


def attention(nc, ident, xa, stats, x, ctx_kv, g_xattn, Wq, bq, Wk, bk, Wv, bv, Wo, bo):
    f32, f32r, i32 = mybir.dt.float32, mybir.dt.float32r, mybir.dt.int32
    ACT, AX = mybir.ActivationFunctionType, mybir.AxisListType

    B, SQ, EMB = x.shape
    SK = ctx_kv.shape[1]
    HEADS, HD = 16, EMB // 16
    KC = 3
    KW = SK // KC
    P = 128
    DC = EMB // P
    PAIRS = HEADS // 2
    SKP = SK + 1
    QW = 2 * SQ
    KQ = SKP + QW
    LN_EPS = 1e-5
    ONE_ROW = 96
    NSLOT = 3

    ctx = ExitStack()
    with ctx:
        def sb(name, shape, dt=f32):
            return ctx.enter_context(nc.sbuf_tensor(name, shape, dt))

        def sem(name):
            return ctx.enter_context(nc.semaphore(name))

        head_rows = sb("head_rows", [P, 8])
        q_mask = sb("q_mask", [P, 2])
        wq_sb, wk_sb, wv_sb, wo_sb = (sb(n, [P, DC, EMB]) for n in ("wq_sb", "wk_sb", "wv_sb", "wo_sb"))
        bq_sb, bk_sb = sb("bq_sb", [P, DC]), sb("bk_sb", [P, DC])
        bv_sb = sb("bv_sb", [P, KC, EMB])
        bo_sb = sb("bo_sb", [SQ, EMB])
        gate_x = sb("gate_x", [SQ, 1])
        tanh_x = sb("tanh_x", [SQ, 1])
        bo_gated = sb("bo_gated", [SQ, EMB])

        mean, var, rstd, ln_tmp = (sb(n, [SQ, B]) for n in ("mean", "var", "rstd", "ln_tmp"))

        ctx_nat = sb("ctx_nat", [KW, NSLOT, KC, EMB])
        ctx_t = sb("ctx_t", [P, NSLOT, DC, SK])
        xn = sb("xn", [SQ, EMB])
        xn_t = sb("xn_t", [P, DC, SQ])
        q_raw = sb("q_raw", [P, DC, SQ])
        q_msk = sb("q_msk", [P, DC, 2, SQ])
        KLO, QHI, KHI, QLO = 0, SKP, KQ, KQ + SKP
        split = sb("split", [P, NSLOT, DC, 2 * KQ], f32r)
        stack = sb("stack", [ONE_ROW + 1, NSLOT, PAIRS, KQ], f32r)
        v_sb = sb("v_sb", [KW, NSLOT, KC, HEADS, 32])
        negmax = sb("negmax", [SQ, 2, 2, 4])
        negmax_t = sb("negmax_t", [8, 2, SQ], f32r)
        probs = sb("probs", [KW, 2, KC, 4 * SQ])
        pv_t = sb("pv_t", [P, 4, SQ])
        rsum = sb("rsum", [SQ, HEADS])
        o_nat = sb("o_nat", [SQ, EMB])
        o_t = sb("o_t", [P, DC, SQ])

        ps = ctx.enter_context(nc.psum_tensor("ps", [P, 8, 512], f32))
        MAXB, EXPB, PVB, MISC = 0, 2, 4, 5

        s_w = sem("s_w")
        s_xload = [sem(f"s_xload{n}") for n in range(4)]
        s_wo = sem("s_wo")
        s_ctx = [sem(f"s_ctx{n}") for n in range(NSLOT)]
        s_stack = [sem(f"s_stack{n}") for n in range(NSLOT)]
        s_nmrow = [[sem(f"s_nmrow{h}{n}") for n in range(NSLOT)] for h in range(2)]
        s_const = sem("s_const")
        s_msk = sem("s_msk")
        s_stats = sem("s_stats")
        s_var, s_std, s_ln = sem("s_var"), sem("s_std"), sem("s_ln")
        s_tanh, s_bog = sem("s_tanh"), sem("s_bog")
        s_ctx_ps, s_ctx_t = sem("s_ctx_ps"), sem("s_ctx_t")
        s_xn, s_xn_ps, s_xn_t = sem("s_xn"), sem("s_xn_ps"), sem("s_xn_t")
        s_k_ps, s_khi, s_klo = sem("s_k_ps"), sem("s_khi"), sem("s_klo")
        s_q_ps, s_q_raw, s_qhi, s_qlo = (sem(n) for n in ("s_q_ps", "s_q_raw", "s_qhi", "s_qlo"))
        s_v_ps, s_v = sem("s_v_ps"), sem("s_v")
        s_max_ps, s_max = sem("s_max_ps"), sem("s_max")
        s_nm_ps, s_nm_t = sem("s_nm_ps"), sem("s_nm_t")
        s_exp_ps, s_exp = sem("s_exp_ps"), sem("s_exp")
        s_pv, s_pv_t = sem("s_pv"), sem("s_pv_t")
        s_ot_ps, s_rsum, s_o_nat = sem("s_ot_ps"), sem("s_rsum"), sem("s_o_nat")
        s_on_ps, s_o_t = sem("s_on_ps"), sem("s_o_t")
        s_o_ps, s_x2 = sem("s_o_ps"), sem("s_x2")
        s_stats2 = sem("s_stats2")
        s_xb = sem("s_xb")
        s_dve_met = sem("s_dve_met")
        s_sp_met = sem("s_sp_met")
        s_settled = sem("s_settled")

        def num(b):
            return NSLOT * b[0] + b[1]

        def batch(i):
            return (i // NSLOT, i % NSLOT)

        def wait(eng, s, v):
            if isinstance(v, int) and v <= 0:
                return
            eng.wait_ge(s, v)

        def pipeline(eng, step):
            def parts(i):
                return tuple(batch(n) if 0 <= n < B else None for n in (i - 1, i, i + 1, i + 2, i + 3))
            first = 2
            for i in range(-3, first):
                step(*parts(i))
            trips = (B - 4 - first) // NSLOT
            with eng.Fori(0, trips) as j:
                for r in range(first - 1, first - 1 + NSLOT):
                    step(*((j + (r + n) // NSLOT, (r + n) % NSLOT) for n in range(5)))
            for i in range(first + trips * NSLOT, B + 1):
                step(*parts(i))

        block = ctx.enter_context(nc.Block())

        @block.sync
        def _(sp):
            def load_ctx(b):
                n = num(b) if isinstance(b[0], int) else sp.snap(num(b), min_val=0, max_val=B - 1)
                wait(sp, s_ctx_ps, DC * (num(b) - NSLOT + 1))
                sp.dma_start(ctx_nat[:, b[1], :, :],
                             ctx_kv[bass.ds(n, 1), :, :].rearrange("b (c p) d -> p (b c) d", p=KW)
                             ).then_inc(s_ctx[b[1]], 16)

            load_ctx(batch(0))
            sp.dma_start(wk_sb[:, :, :], Wk.rearrange("(k p) n -> p k n", p=P)).then_inc(s_w, 16)
            sp.dma_start(bk_sb[:, :], bk.rearrange("(k p) -> p k", p=P), allow_slow_non_contiguous=True).then_inc(s_w, 16)
            sp.dma_start(bq_sb[:, :], bq.rearrange("(k p) -> p k", p=P), allow_slow_non_contiguous=True).then_inc(s_w, 16)
            sp.dma_start(wq_sb[:, :, :], Wq.rearrange("(k p) n -> p k n", p=P)).then_inc(s_w, 16)
            sp.dma_start(wv_sb[:, :, :], Wv.rearrange("(k p) n -> p k n", p=P)).then_inc(s_w, 16)
            sp.dma_start(bv_sb[:, :, :], bv.rearrange("(o c d) -> o c d", o=1, c=1).broadcast_to([P, KC, EMB])).then_inc(s_w, 16)

            def step(e, b, c, s, a):
                if s:
                    wait(sp, s_exp_ps, 12 * (num(s) - NSLOT + 1))
                    sp.sem_inc(s_sp_met, 1)
                    wait(sp, s_klo, DC * (num(s) + 1))
                    sp.sem_inc(s_sp_met, 1)
                    wait(sp, s_qlo, num(s) + 1)
                    src, dst = split[:, s[1], :, :].bitcast(f32), stack[:, s[1], :, :].bitcast(f32)
                    for g in range(4):
                        rows, pr = slice(32 * g, 32 * g + 32), slice(DC * g, DC * g + DC)
                        sp.dma_start(dst[0:32, pr, 0:SKP], src[rows, :, KHI:KHI + SKP]).then_inc(s_stack[s[1]], 16)
                        sp.dma_start(dst[0:32, pr, SKP:KQ], src[rows, :, QHI:QHI + QW]).then_inc(s_stack[s[1]], 16)
                        sp.dma_start(dst[32:64, pr, :], src[rows, :, KLO:KLO + KQ]).then_inc(s_stack[s[1]], 16)
                        sp.dma_start(dst[64:96, pr, :], src[rows, :, KHI:KHI + KQ]).then_inc(s_stack[s[1]], 16)
                if a and not (isinstance(a[0], int) and num(a) == B - 1):
                    q, r = (a[0] + (a[1] + 1) // NSLOT, (a[1] + 1) % NSLOT)
                    load_ctx((q, r))

            pipeline(sp, step)

        @block.gpsimd
        def _(gp):
            gp.memset(ident[:, :], 0.0).then_inc(s_const, 1)
            gp.memset(head_rows[:, :], 1.0).then_inc(s_const, 1)
            gp.wait_ge(s_const, 2)
            gp.affine_select(out=ident[:, :], in_=ident[:, :], compare_op=ALU.not_equal, fill=1.0, base=0,
                             pattern=[[-1, P]], channel_multiplier=1).then_inc(s_const, 1)
            gp.affine_select(out=head_rows[:, :], in_=head_rows[:, :], compare_op=ALU.is_ge, fill=0.0, base=0,
                             pattern=[[-HD, 8]], channel_multiplier=1).then_inc(s_const, 1)
            gp.wait_ge(s_const, 4)
            gp.affine_select(out=head_rows[:, :], in_=head_rows[:, :], compare_op=ALU.is_ge, fill=0.0, base=HD - 1,
                             pattern=[[HD, 8]], channel_multiplier=-1).then_inc(s_const, 1)

            gp.wait_ge(s_bog, 1)
            gp.wait_ge(s_ln, 1)
            gp.wait_ge(s_msk, 2)

            def settle():
                gp.sem_inc(s_settled, 1)

            def nm_rows(c, half):
                wait(gp, s_nm_t, 2 * num(c) + half + 1)
                wait(gp, s_exp_ps, 12 * (num(c) - NSLOT + 1))
                settle()
                dst = stack[ONE_ROW:ONE_ROW + 1, c[1], 4 * half:4 * half + 4, :].bitcast(f32)
                for h in range(2):
                    gp.dma_start(dst[:, :, SKP + SQ * h:SKP + SQ * h + SQ],
                                 negmax_t[4 * h:4 * h + 4, half, :].bitcast(f32)).then_inc(s_nmrow[half][c[1]], 16)

            def step(e, b, c, s, a):
                if a:
                    n = num(a)
                    wait(gp, s_xn, n + 1)
                    xrow = xa[:, bass.ds(n, 1), :].rearrange("p b d -> p (b d)")
                    gp.tensor_tensor(xrow, xrow, bo_gated[:, :], ALU.add).then_inc(s_xb, 1)
                if c:
                    nm_rows(c, 0)
                if a:
                    wait(gp, s_q_raw, n + 1)
                    wait(gp, s_qlo, n)
                    wait(gp, s_stack[a[1]], 256 * a[0])
                    for h in range(2):
                        mask = q_mask[:, h:h + 1].broadcast_to([P, DC * SQ]).rearrange("p (k q) -> p k q", k=DC)
                        gp.tensor_tensor(q_msk[:, :, h, :], q_raw[:, :, :], mask, ALU.mult)
                        last = gp.tensor_tensor(split[:, a[1], :, QHI + SQ * h:QHI + SQ * h + SQ], q_raw[:, :, :], mask, ALU.mult)
                    last.then_inc(s_qhi, 1)
                    wait(gp, s_qhi, n + 1)
                    gp.tensor_tensor(split[:, a[1], :, QLO:QLO + QW], q_msk[:, :, :, :].rearrange("p k h q -> p k (h q)"),
                                     split[:, a[1], :, QHI:QHI + QW].bitcast(f32), ALU.subtract).then_inc(s_qlo, 1)
                if c:
                    nm_rows(c, 1)

            pipeline(gp, step)

        @block.scalar
        def _(act):
            act.dma_start(gate_x[:, :], g_xattn.rearrange("(a b) -> a b", a=1).broadcast_to([SQ, 1])).then_inc(s_wo, 16)
            for n in range(4):
                act.dma_start(xa[:, 8 * n:8 * n + 8, :], x[8 * n:8 * n + 8, :, :].rearrange("b q d -> q b d")).then_inc(s_xload[n], 16)
            act.dma_start(bo_sb[:, :], bo.rearrange("(a b) -> a b", a=1).broadcast_to([SQ, EMB])).then_inc(s_wo, 16)
            for g in range(2):
                for m in range(2):
                    act.dma_start(wo_sb[64 * g + 32 * m:64 * g + 32 * m + 32, :, :],
                                  Wo.rearrange("(m k g r) n -> m g r k n", m=2, k=2, g=2)[m, g, :, :, :]).then_inc(s_wo, 16)
            act.wait_ge(s_var, 1)
            act.activation(ln_tmp[:, :], var[:, :], ACT.Sqrt).then_inc(s_std, 1)
            act.wait_ge(s_wo, 16 * 6)
            act.activation(tanh_x[:, :], gate_x[:, :], ACT.Tanh).then_inc(s_tanh, 1)

            def step(e, b, c, s, a):
                for k in range(12):
                    if b:
                        g, ch = k // 3, k % 3
                        wait(act, s_exp_ps, 12 * num(b) + k + 1)
                        if ch == 0:
                            wait(act, s_pv, 4 * num(b) + g - 1)
                        act.activation(probs[:, g % 2, ch, :], ps[0:KW, EXPB + k % 2, 0:4 * SQ], ACT.Exp).then_inc(s_exp, 1)
                    if k == 1 and e:
                        wait(act, s_pv, 4 * num(e) + 4)
                        wait(act, s_ot_ps, num(e))
                        act.activation(pv_t[:, :, :], ps[:, PVB, 0:4 * SQ], ACT.Copy).then_inc(s_pv_t, 1)
                    if k in (0, 1) and a:
                        wait(act, s_ctx_ps, DC * num(a) + k + 1)
                        wait(act, s_v_ps, 2 * (num(a) - NSLOT + 1))
                        act.activation(ctx_t[:, a[1], k, :], ps[:, MISC + k, 0:SK], ACT.Copy).then_inc(s_ctx_t, 1)
                    if k == 2 and a:
                        wait(act, s_xn_ps, num(a) + 1)
                        wait(act, s_q_ps, num(a))
                        act.activation(xn_t[:, :, :], ps[:, MISC + 2, 0:DC * SQ], ACT.Copy).then_inc(s_xn_t, 1)
                    if k in (4, 8) and a:
                        m = (k - 4) // 4
                        wait(act, s_k_ps, DC * num(a) + m + 1)
                        wait(act, s_stack[a[1]], 256 * a[0])
                        act.activation(split[:, a[1], m, KHI:KHI + SK], ps[:, MISC + 1 + m, 0:SK], ACT.Identity,
                                       bias=bk_sb[:, m:m + 1]).then_inc(s_khi, 1)
                    if k == 5 and a:
                        wait(act, s_q_ps, num(a) + 1)
                        wait(act, s_qhi, num(a))
                        for m in range(DC):
                            last = act.activation(q_raw[:, m, :], ps[:, MISC + 2, SQ * m:SQ * m + SQ], ACT.Identity,
                                                  bias=bq_sb[:, m:m + 1])
                        last.then_inc(s_q_raw, 1)
                    if k in (6, 11) and c:
                        half = k // 11
                        wait(act, s_nm_ps, 2 * num(c) + half + 1)
                        p = (c[0] + (c[1] + 2) // NSLOT - 1, (c[1] + 2) % NSLOT)
                        wait(act, s_nmrow[half][p[1]], 32 * (p[0] + 1))
                        act.activation(negmax_t[:, half, :], ps[0:8, MISC, 0:SQ], ACT.Copy).then_inc(s_nm_t, 1)
                    if k == 7 and e:
                        wait(act, s_on_ps, num(e) + 1)
                        wait(act, s_o_ps, num(e))
                        act.activation(o_t[:, :, :], ps[:, MISC + 1, 0:DC * SQ], ACT.Copy).then_inc(s_o_t, 1)

            pipeline(act, step)

        def layer_norm_stats(dve, link):
            me, mo = stats[:, :, 1], stats[:, :, 4]
            link(dve.tensor_tensor(mean[:, :], me, mo, ALU.add))
            link(dve.tensor_tensor(ln_tmp[:, :], me, mo, ALU.subtract))
            link(dve.tensor_tensor(ln_tmp[:, :], ln_tmp[:, :], ln_tmp[:, :], ALU.mult))
            link(dve.tensor_tensor(var[:, :], stats[:, :, 2], stats[:, :, 5], ALU.add))
            link(dve.tensor_scalar(var[:, :], var[:, :], 1.0 / EMB, LN_EPS, ALU.mult, ALU.add))
            link(dve.tensor_scalar(mean[:, :], mean[:, :], 0.5, None, ALU.mult))
            dve.scalar_tensor_tensor(out=var[:, :], in0=ln_tmp[:, :], scalar=0.25, in1=var[:, :], op0=ALU.mult,
                                     op1=ALU.add).then_inc(s_var, 1)
            dve.wait_ge(s_std, 1)
            link(dve.reciprocal(rstd[:, :], ln_tmp[:, :]))
            link(dve.tensor_tensor(ln_tmp[:, :], rstd[:, :], rstd[:, :], ALU.mult))
            link(dve.tensor_tensor(ln_tmp[:, :], ln_tmp[:, :], var[:, :], ALU.mult))
            link(dve.tensor_scalar(ln_tmp[:, :], ln_tmp[:, :], -0.5, 1.5, ALU.mult, ALU.add))
            dve.tensor_tensor(rstd[:, :], rstd[:, :], ln_tmp[:, :], ALU.mult).then_inc(s_ln, 1)
            dve.wait_ge(s_ln, 1)

        @block.vector
        def _(dve):
            chain = [0]

            def link(ins):
                chain[0] += 1
                ins.then_inc(s_stats, 1)
                dve.wait_ge(s_stats, chain[0])

            dve.memset(stack[ONE_ROW:ONE_ROW + 1, :, :, 0:SKP].bitcast(f32), 1.0)
            for m in (KLO, KHI):
                dve.memset(split[:, :, :, m + SK:m + SKP].bitcast(f32), 0.0)
            dve.memset(v_sb[:, :, :, :, HD:HD + 1], 1.0)
            dve.memset(v_sb[:, :, :, :, HD + 1:32], 0.0).then_inc(s_msk, 1)
            dve.wait_ge(s_const, 5)
            dve.tensor_reduce(q_mask[:, :], head_rows[:, :].rearrange("p (g h) -> p h g", h=2), axis=AX.X, op=ALU.add).then_inc(s_stats, 1)
            chain[0] += 1
            dve.wait_ge(s_stats, chain[0])
            dve.tensor_scalar(q_mask[:, :], q_mask[:, :], float(HD) ** -0.5, None, ALU.mult).then_inc(s_msk, 1)
            for n in range(4):
                dve.wait_ge(s_xload[n], 16)
                for i in range(8 * n, 8 * n + 8):
                    last = dve.bn_stats(stats[:, i, :], xa[:, i, :])
            link(last)
            layer_norm_stats(dve, link)
            dve.wait_ge(s_wo, 16 * 6)
            dve.wait_ge(s_tanh, 1)
            dve.tensor_scalar(bo_gated[:, :], bo_sb[:, :], tanh_x[:, :], None, ALU.mult).then_inc(s_bog, 1)
            dve.wait_ge(s_w, 16 * 6)

            def step(e, b, c, s, a):
                if a:
                    n = num(a)
                    wait(dve, s_xn_ps, n)
                    dve.tensor_scalar(xn[:, :], xa[:, bass.ds(n, 1), :].rearrange("p b d -> p (b d)"), mean[:, bass.ds(n, 1)],
                                      rstd[:, bass.ds(n, 1)], ALU.subtract, ALU.mult).then_inc(s_xn, 1)
                for k in range(12):
                    if k % 3 != 2 and c:
                        t = k // 3 * 2 + k % 3
                        half, p4 = t // 4, t % 4
                        wait(dve, s_max_ps, 8 * num(c) + t + 1)
                        if p4 == 0:
                            wait(dve, s_nm_ps, 2 * num(c) + half - 1)
                        dve.tensor_reduce(negmax[:, half, :, p4], ps[0:SQ, MAXB:MAXB + 2, 0:SK],
                                          axis=AX.X, op=ALU.max, negate=True).then_inc(s_max, 1)
                    if k == 3 and e:
                        wait(dve, s_ot_ps, num(e) + 1)
                        heads = ps[0:SQ, MISC, :].rearrange("p (h c) -> p h c", c=32)
                        dve.reciprocal(rsum[:, :], heads[:, :, HD]).then_inc(s_rsum, 1)
                        wait(dve, s_rsum, num(e) + 1)
                        wait(dve, s_on_ps, num(e))
                        dve.tensor_tensor(o_nat[:, :].rearrange("p (h d) -> p h d", d=HD), heads[:, :, 0:HD],
                                          rsum[:, :].rearrange("p (h o) -> p h o", o=1).broadcast_to([SQ, HEADS, HD]), ALU.mult).then_inc(s_o_nat, 1)
                    if k in (4, 8) and a:
                        m = (k - 4) // 4
                        wait(dve, s_khi, DC * num(a) + m + 1)
                        wait(dve, s_stack[a[1]], 256 * a[0])
                        dve.scalar_tensor_tensor(out=split[:, a[1], m, KLO:KLO + SK], in0=ps[:, MISC + 1 + m, 0:SK], scalar=bk_sb[:, m:m + 1],
                                                 in1=split[:, a[1], m, KHI:KHI + SK].bitcast(f32), op0=ALU.add,
                                                 op1=ALU.subtract).then_inc(s_klo, 1)
                    if k == 9 and e:
                        wait(dve, s_o_ps, num(e) + 1)
                        wait(dve, s_xb, num(e) + 1)
                        xrow = xa[:, bass.ds(num(e), 1), :].rearrange("p b d -> p (b d)")
                        dve.scalar_tensor_tensor(out=xrow, in0=ps[0:SQ, MISC, 0:EMB], scalar=tanh_x[:, :], in1=xrow,
                                                 op0=ALU.mult, op1=ALU.add).then_inc(s_x2, 1)
                        wait(dve, s_x2, num(e) + 1)
                        dve.sem_inc(s_dve_met, 1)
                        dve.bn_stats(stats[:, bass.ds(num(e), 1), :].rearrange("p b s -> p (b s)"), xrow).then_inc(s_stats2, 1)
                    if k in (10, 11) and s:
                        h = k - 10
                        nch = KC - 1 if h == 0 else 1
                        wait(dve, s_v_ps, 2 * num(s) + h + 1)
                        wait(dve, s_pv, 4 * (num(s) - NSLOT + 1))
                        dve.tensor_tensor(v_sb[:, s[1], 2 * h:2 * h + nch, :, 0:HD].rearrange("p c h d -> p (c h) d"),
                                          ps[0:KW, MISC + 1 + h, 0:nch * EMB].rearrange("p (h d) -> p h d", d=HD),
                                          bv_sb[0:KW, 0:nch, :].rearrange("p c (h d) -> p (c h) d", d=HD), ALU.add).then_inc(s_v, 1)

            pipeline(dve, step)

        @block.tensor
        def _(pe):
            pe.wait_ge(s_const, 3)
            pe.wait_ge(s_w, 16 * 6)
            pe.wait_ge(s_wo, 16 * 6)
            pe.wait_ge(s_msk, 2)

            def probs_scores(b, k):
                g, ch = k // 3, k % 3
                if ch == 0 and g % 2 == 0:
                    wait(pe, s_nmrow[g // 2][b[1]], 32 * (b[0] + 1))
                wait(pe, s_exp, 12 * num(b) + k - 1)
                for m in range(2):
                    p = 2 * g + m
                    last = pe.matmul(ps[0:KW, EXPB + k % 2, QW * m:QW * m + QW],
                                     stack[:, b[1], p, KW * ch:KW * ch + KW], stack[:, b[1], p, SKP:KQ], start=True, stop=True)
                last.then_inc(s_exp_ps, 1)

            def values(b, g):
                wait(pe, s_exp, 12 * num(b) + 3 * g + 3)
                if g == 0:
                    wait(pe, s_v, 2 * (num(b) + 1))
                    wait(pe, s_pv_t, num(b))
                for ch in range(KC):
                    for j in range(4):
                        head = 8 * (j // 2) + 2 * g + j % 2
                        last = pe.matmul(ps[32 * j:32 * j + 32, PVB, SQ * g:SQ * g + SQ], v_sb[:, b[1], ch, head, :],
                                         probs[:, g % 2, ch, SQ * j:SQ * j + SQ], start=(ch == 0), stop=(ch == KC - 1))
                last.then_inc(s_pv, 1)

            def max_scores(c, t):
                if t == 0:
                    wait(pe, s_stack[c[1]], 256 * (c[0] + 1))
                wait(pe, s_max, 8 * num(c) + t)
                for h in range(2):
                    last = pe.matmul(ps[0:SQ, MAXB + h, 0:SKP], stack[0:ONE_ROW, c[1], t, SKP + SQ * h:SKP + SQ * h + SQ],
                                     stack[0:ONE_ROW, c[1], t, 0:SKP], start=True, stop=True)
                last.then_inc(s_max_ps, 1)

            def step(e, b, c, s, a):
                first = e is None
                for k in range(12):
                    if b:
                        probs_scores(b, k)
                    if k == 1 and e:
                        values(e, 3)
                    if k % 3 == 1 and k > 1 and b:
                        values(b, k // 3 - 1)
                    if k % 3 != 2 and c:
                        max_scores(c, k // 3 * 2 + k % 3)
                    if k in (0, 1) and a:
                        if k == 0:
                            wait(pe, s_nm_t, 2 * (num(a) - 2))
                        else:
                            wait(pe, s_v, 2 * (num(a) - 2) + 1)
                            if first:
                                wait(pe, s_klo, DC * num(a) - 1)
                        wait(pe, s_ctx[a[1]], 16 * (a[0] + 1))
                        for ch in range(KC):
                            last = pe.transpose(ps[:, MISC + k, KW * ch:KW * ch + KW], ctx_nat[:, a[1], ch, P * k:P * k + P], ident[0:KW, 0:KW])
                        last.then_inc(s_ctx_ps, 1)
                    if k == 2 and a:
                        wait(pe, s_v, 2 * (num(a) - 1))
                        if first:
                            wait(pe, s_klo, DC * num(a))
                        wait(pe, s_xn, num(a) + 1)
                        for m in range(DC):
                            last = pe.transpose(ps[:, MISC + 2, SQ * m:SQ * m + SQ], xn[:, P * m:P * m + P], ident[0:SQ, 0:SQ])
                        last.then_inc(s_xn_ps, 1)
                    if k == 3 and e:
                        if a:
                            wait(pe, s_ctx_t, DC * num(a) + 1)
                        else:
                            wait(pe, s_nm_t, 2 * min(num(e) + 2, B))
                            wait(pe, s_x2, num(e))
                        wait(pe, s_pv_t, num(e) + 1)
                        for g in range(4):
                            last = pe.transpose(ps[0:SQ, MISC, P * g:P * g + P], pv_t[:, g, :], ident[:, :])
                        last.then_inc(s_ot_ps, 1)
                    if k in (4, 8) and a:
                        m = (k - 4) // 4
                        if m == 0:
                            wait(pe, s_ctx_t, DC * (num(a) + 1))
                        else:
                            wait(pe, s_q_raw, num(a) + 1)
                        for n in range(DC):
                            last = pe.matmul(ps[:, MISC + 1 + m, 0:SK], wk_sb[:, n, P * m:P * m + P], ctx_t[:, a[1], n, :],
                                             start=(n == 0), stop=(n == DC - 1))
                        last.then_inc(s_k_ps, 1)
                    if k == 5 and a:
                        wait(pe, s_xn_t, num(a) + 1)
                        for m in range(DC):
                            for n in range(DC):
                                last = pe.matmul(ps[:, MISC + 2, SQ * m:SQ * m + SQ], wq_sb[:, n, P * m:P * m + P], xn_t[:, n, :],
                                                 start=(n == 0), stop=(n == DC - 1))
                        last.then_inc(s_q_ps, 1)
                    if k == 6 and c:
                        negmax_transpose(e, c, 0)
                    if k == 7 and e:
                        if a:
                            wait(pe, s_klo, DC * num(a) + 1)
                        else:
                            wait(pe, s_v, 2 * min(num(e) + 2, B - 1) + 1)
                        wait(pe, s_o_nat, num(e) + 1)
                        for m in range(DC):
                            last = pe.transpose(ps[:, MISC + 1, SQ * m:SQ * m + SQ], o_nat[:, P * m:P * m + P], ident[0:SQ, 0:SQ])
                        last.then_inc(s_on_ps, 1)
                    if k == 9 and e:
                        if c:
                            wait(pe, s_nm_t, 2 * num(c) + 1)
                        wait(pe, s_o_t, num(e) + 1)
                        for n in range(DC):
                            last = pe.matmul(ps[0:SQ, MISC, 0:EMB], o_t[:, n, :], wo_sb[:, n, :], start=(n == 0), stop=(n == DC - 1))
                        last.then_inc(s_o_ps, 1)
                    if k in (10, 11) and s:
                        h = k - 10
                        if first and a:
                            wait(pe, s_klo, DC * num(a) + 1)
                        if h == 1:
                            if a:
                                wait(pe, s_klo, DC * (num(a) + 1))
                            else:
                                wait(pe, s_v, 2 * num(s))
                        for ch in ((0, 1), (2,))[h]:
                            for n in range(DC):
                                last = pe.matmul(ps[0:KW, MISC + 1 + h, EMB * (ch % 2):EMB * (ch % 2) + EMB], ctx_t[:, s[1], n, KW * ch:KW * ch + KW],
                                                 wv_sb[:, n, :], start=(n == 0), stop=(n == DC - 1))
                        last.then_inc(s_v_ps, 1)
                if c:
                    negmax_transpose(e, c, 1)

            def negmax_transpose(e, c, half):
                wait(pe, s_max, 8 * num(c) + 4 * half + 4)
                if e:
                    wait(pe, s_x2 if half else s_o_nat, num(e) + 1)
                elif half:
                    wait(pe, s_nm_t, 2 * num(c) + 1)
                pe.transpose(ps[0:8, MISC, 0:SQ], negmax[:, half, :, :].rearrange("p a b -> p (a b)"), ident[0:SQ, 0:SQ]).then_inc(s_nm_ps, 1)

            pipeline(pe, step)


def route_and_ffn(nc, ident, xa, stats, g_ffn, w_router, w1, w2, w3, out):
    f32, i32 = mybir.dt.float32, mybir.dt.int32
    ACT, AX = mybir.ActivationFunctionType, mybir.AxisListType
    P = 128
    SQ, B, EMB = xa.shape
    NE, _, F = w1.shape
    DC = EMB // P
    TOK = B * SQ
    TOP = 2
    FC = (F + P - 1) // P
    F_LAST = F - (FC - 1) * P
    TILES = TOP * TOK // P + NE - 1
    TW = 64
    PER_E = TOK // P
    MAGIC = 12582912.0
    LN_EPS = 1e-5
    NS = 3
    NX = 4

    xn_dram = nc.dram_tensor("xn_scratch", (TOK, EMB), f32, kind="Internal").ap()
    y_dram = nc.dram_tensor("y_scratch", (TOP * TOK + TW * P, EMB), f32, kind="Internal").ap()

    ctx = ExitStack()
    with ctx:
        def sb(name, shape, dt=f32):
            return ctx.enter_context(nc.sbuf_tensor(name, shape, dt))

        def sem(name):
            return ctx.enter_context(nc.semaphore(name))

        w1_sb = sb("w1_sb", [P, DC, NE, F])
        w3_sb = sb("w3_sb", [P, DC, NE, F])
        w2_sb = sb("w2_sb", [P, FC, NE, EMB])
        wr_sb = sb("wr_sb", [NE, EMB])
        wr_t = sb("wr_t", [P, DC, NE])
        gate_f = sb("gate_f", [SQ, 1])
        tanh_f = sb("tanh_f", [SQ, 1])
        mean, var, rstd, ln_tmp = (sb(n, [SQ, B]) for n in ("mean2", "var2", "rstd2", "ln_tmp2"))
        xn = sb("xn2", [SQ, NX, EMB])
        xn_t = sb("xn2_t", [P, NX, DC, SQ])
        probs, mask1, mask2, both, tmp = (sb(n, [SQ, B, NE]) for n in ("r_probs", "r_mask1", "r_mask2", "r_both", "r_tmp"))
        totals, cum_a, cum_b, slot_e = (sb(n, [SQ, B, NE]) for n in ("r_totals", "r_cum_a", "r_cum_b", "r_slot_e"))
        col = sb("r_col", [SQ, B])
        gates, slots, tile_no, row_no, value = (sb(n, [SQ, TOP, B]) for n in ("r_gates", "r_slots", "r_tile", "r_row", "r_value"))
        value_i = sb("value_i", [SQ, TOP, B], i32)
        cmp = sb("r_cmp", [SQ, NE, PER_E])
        n_tiles, ct_a, ct_b, base = (sb(n, [SQ, NE]) for n in ("r_ntiles", "r_ct_a", "r_ct_b", "r_base"))
        first_e = sb("first_e", [SQ, NE])
        thresh = sb("thresh", [SQ, PER_E])
        iota_c, iota_ci = sb("iota_c", [P, P]), sb("iota_ci", [P, P], i32)
        iota_p, iota_pi = sb("iota_p", [P, TW]), sb("iota_pi", [P, TW], i32)
        before = sb("before", [SQ, SQ])
        ones = sb("ones", [SQ, SQ])
        one_row = sb("one_row", [SQ, 2, P])
        one_val = sb("one_val", [SQ, 2, 2, TW])
        zeros = sb("zeros", [SQ, P])
        e_cmp = sb("e_cmp", [1, TW, NE])
        e_tile = sb("e_tile", [1, TW])
        e_idx = sb("e_idx", [1, TW], i32)
        t_dst, t_src, t_pad, gate_s = (sb(n, [P, TW]) for n in ("t_dst", "t_src", "t_pad", "gate_s"))
        dst_idx, src_idx = sb("dst_idx", [P, TW], i32), sb("src_idx", [P, TW], i32)
        idx_g, idx_y = sb("idx_g", [P, NS, 1], i32), sb("idx_y", [P, NS, 1], i32)
        xg = sb("xg", [P, NS, EMB])
        xg_t = sb("xg_t", [P, NS, DC, P])
        silu = sb("silu", [P, F])
        h = sb("h", [P, FC * P])
        h_t = sb("h_t", [P, FC, P])
        y = sb("y", [P, NS, EMB])
        yk = sb("yk", [SQ, 2, 4, TOP * EMB])

        ps = ctx.enter_context(nc.psum_tensor("ps2", [P, 8, 512], f32))
        LOGIT, RANK, TABLE = 4, 5, 6
        XTB, AB, BB, HTB, YB = 0, 1, 2, 3, 7

        s_w = sem("f_w")
        s_wr = sem("f_wr")
        s_iota, s_shape = sem("f_iota"), sem("f_shape")
        s_wr_ps, s_wr_t = sem("f_wr_ps"), sem("f_wr_t")
        s_chain = sem("f_chain")
        s_var, s_std, s_tanh, s_silu_tab = sem("f_var"), sem("f_std"), sem("f_tanh"), sem("f_silu_tab")
        s_xn, s_xn_ps, s_xn_t, s_logit = sem("f_xn"), sem("f_xn_ps"), sem("f_xn_t"), sem("f_logit")
        s_xst = [sem(f"f_xst{n}") for n in range(NX)]
        s_shift, s_exp = sem("f_shift"), sem("f_exp")
        s_both, s_rank = sem("f_both"), sem("f_rank")
        s_onehot, s_table = sem("f_onehot"), sem("f_table")
        s_tables = sem("f_tables")
        s_idx, s_xg_ps, s_xg_t = sem("f_idx"), sem("f_xg_ps"), sem("f_xg_t")
        s_xg = [sem(f"f_xg{n}") for n in range(NS)]
        s_yout = [sem(f"f_yout{n}") for n in range(NS)]
        s_a, s_b, s_silu, s_h, s_h_ps, s_h_t, s_y_ps, s_y = (sem(f"f_{n}") for n in ("a", "b", "silu", "h", "h_ps", "h_t", "y_ps", "y"))
        s_met = sem("f_met")
        s_yk = [sem(f"f_yk{n}") for n in range(2)]
        s_add, s_res, s_out = sem("f_add"), sem("f_res"), sem("f_out")

        def num(t):
            return NS * t[0] + t[1]

        def wait(eng, s, v):
            if isinstance(v, int) and v <= 0:
                return
            eng.wait_ge(s, v)

        def pipeline(eng, step):
            def parts(i):
                return tuple((n // NS, n % NS) if 0 <= n < TILES else None for n in (i - 1, i, i + 1, i + 2))
            first = NS + 1
            for i in range(-2, first):
                step(*parts(i))
            trips = (TILES - 2 - first) // NS
            with eng.Fori(0, trips) as j:
                for r in range(first - 1, first - 1 + NS):
                    step(*((j + (r + n) // NS, (r + n) % NS) for n in range(4)))
            for i in range(first + trips * NS, TILES + 1):
                step(*parts(i))

        def looped(eng, count, body):
            body(0)
            with eng.Fori(1, count) as j:
                body(j)

        block = ctx.enter_context(nc.Block())

        @block.sync
        def _(sp):
            def store_group(sp, g):
                sp.wait_ge(s_add, g + 1)
                sp.dma_start(out[4 * g:4 * g + 4, :, :].rearrange("b q d -> q b d"), xa[:, 4 * g:4 * g + 4, :]).then_inc(s_out, 16)

            sp.dma_start(wr_sb[:, :], w_router).then_inc(s_wr, 16)
            sp.dma_start(gate_f[:, :], g_ffn.rearrange("(a b) -> a b", a=1).broadcast_to([SQ, 1])).then_inc(s_wr, 16)
            for k in range(DC):
                for src, dst in ((w1, w1_sb), (w3, w3_sb)):
                    sp.dma_start(dst[:, k, :, :], src[:, P * k:P * k + P, :].rearrange("e p f -> p e f")).then_inc(s_w, 16)
            for c in range(FC):
                n = min(P, F - P * c)
                sp.dma_start(w2_sb[0:n, c, :, :], w2[:, P * c:P * c + n, :].rearrange("e p d -> p e d")).then_inc(s_w, 16)
            with sp.Fori(0, B // NX) as j:
                for u in range(NX):
                    wait(sp, s_xn, NX * j + u + 1)
                    sp.dma_start(xn_dram.rearrange("(j u q) d -> j u q d", u=NX, q=SQ)[bass.ds(j, 1), u, :, :].rearrange("j q d -> q (j d)"),
                                 xn[:, u, :]).then_inc(s_xst[u], 16)
            for n in range(NS):
                wait(sp, s_yout[n], 16 * len(range(n, TILES, NS)))
            yv = y_dram[0:TOP * TOK, :].rearrange("(b q k) d -> q b (k d)", q=SQ, k=TOP)
            for g in range(B // 4):
                wait(sp, s_add, g - 1)
                sp.dma_start(yk[:, g % 2, :, :], yv[:, 4 * g:4 * g + 4, :]).then_inc(s_yk[g % 2], 16)
                if g:
                    store_group(sp, g - 1)
            store_group(sp, B // 4 - 1)
            sp.wait_ge(s_out, 16 * (B // 4))

        @block.gpsimd
        def _(gp):
            gp.iota(iota_ci[:, :], pattern=[[1, P]], base=0, channel_multiplier=0).then_inc(s_iota, 1)
            gp.iota(iota_pi[:, :], pattern=[[P, TW]], base=0, channel_multiplier=1).then_inc(s_iota, 1)
            gp.iota(value_i[:, :, :], pattern=[[1, TOP], [TOP * SQ, B]], base=-TOP * TOK, channel_multiplier=TOP).then_inc(s_iota, 1)
            gp.memset(before[:, :], 1.0).then_inc(s_shape, 1)
            gp.memset(ones[:, :], 1.0).then_inc(s_shape, 1)
            gp.memset(zeros[:, :], 0.0).then_inc(s_shape, 1)
            gp.memset(h[:, F:FC * P], 0.0).then_inc(s_shape, 1)
            gp.wait_ge(s_shape, 4)
            gp.affine_select(out=before[:, :], in_=before[:, :], compare_op=ALU.is_gt, fill=0.0, base=0,
                             pattern=[[1, SQ]], channel_multiplier=-1).then_inc(s_shape, 1)
            gp.wait_ge(s_tables, 1)
            for n in range(NX):
                gp.wait_ge(s_xst[n], 16 * (B // NX))

            def settle():
                gp.sem_inc(s_met, 1)

            def step(o, m, x, g):
                if g:
                    wait(gp, s_idx, num(g) + 1)
                    wait(gp, s_xg_ps, num(g) - NS + 1)
                    settle()
                    gp.indirect_dma_start(xg[:, g[1], :], None, xn_dram, bass.IndirectOffsetOnAxis(ap=idx_g[:, g[1], :], axis=0)
                                          ).then_inc(s_xg[g[1]], 16)
                if o:
                    wait(gp, s_y, num(o) + 1)
                    settle()
                    gp.indirect_dma_start(y_dram, bass.IndirectOffsetOnAxis(ap=idx_y[:, o[1], :], axis=0), y[:, o[1], :], None
                                          ).then_inc(s_yout[o[1]], 16)

            pipeline(gp, step)

        @block.scalar
        def _(act):
            act.wait_ge(s_var, 1)
            act.activation(ln_tmp[:, :], var[:, :], ACT.Sqrt).then_inc(s_std, 1)
            act.wait_ge(s_wr, 32)
            act.activation(tanh_f[:, :], gate_f[:, :], ACT.Tanh).then_inc(s_tanh, 1)
            def turned(j):
                for u in range(NX):
                    b = NX * j + u
                    wait(act, s_xn_ps, b + 1)
                    wait(act, s_logit, NX * j)
                    act.activation(xn_t[:, u, :, :], ps[:, u, 0:DC * SQ], ACT.Copy).then_inc(s_xn_t, 1)

            looped(act, B // NX, turned)
            act.wait_ge(s_shift, 1)
            act.activation(probs[:, :, :], tmp[:, :, :], ACT.Exp).then_inc(s_exp, 1)
            act.wait_ge(s_tables, 1)

            def step(o, m, x, g):
                if m:
                    wait(act, s_a, num(m) + 1)
                    wait(act, s_h, num(m))
                    act.activation(silu[:, :], ps[:, AB, 0:F], ACT.Silu).then_inc(s_silu, 1)
                if o:
                    wait(act, s_h_ps, num(o) + 1)
                    wait(act, s_y_ps, num(o))
                    act.activation(h_t[:, :, :], ps[:, HTB, 0:FC * P], ACT.Copy).then_inc(s_h_t, 1)
                if x:
                    wait(act, s_xg_ps, num(x) + 1)
                    wait(act, s_b, num(x) - NS + 1)
                    act.activation(xg_t[:, x[1], :, :], ps[:, XTB, 0:DC * P], ACT.Copy).then_inc(s_xg_t, 1)

            pipeline(act, step)

        @block.vector
        def _(dve):
            chain = [0]

            def link(ins):
                chain[0] += 1
                ins.then_inc(s_chain, 1)
                dve.wait_ge(s_chain, chain[0])

            def bcast(ap, shape, at):
                return (ap.rearrange("p (n o) -> p n o", o=1) if at == 2 else ap.rearrange("p (o n) -> p o n", o=1)).broadcast_to(shape)

            me, mo = stats[:, :, 1], stats[:, :, 4]
            link(dve.tensor_tensor(mean[:, :], me, mo, ALU.add))
            link(dve.tensor_tensor(ln_tmp[:, :], me, mo, ALU.subtract))
            link(dve.tensor_tensor(ln_tmp[:, :], ln_tmp[:, :], ln_tmp[:, :], ALU.mult))
            link(dve.tensor_tensor(var[:, :], stats[:, :, 2], stats[:, :, 5], ALU.add))
            link(dve.tensor_scalar(var[:, :], var[:, :], 1.0 / EMB, LN_EPS, ALU.mult, ALU.add))
            link(dve.tensor_scalar(mean[:, :], mean[:, :], 0.5, None, ALU.mult))
            dve.scalar_tensor_tensor(out=var[:, :], in0=ln_tmp[:, :], scalar=0.25, in1=var[:, :], op0=ALU.mult, op1=ALU.add).then_inc(s_var, 1)
            dve.wait_ge(s_wr_ps, 1)
            dve.tensor_copy(wr_t[:, :, :], ps[:, 0, 0:DC * NE]).then_inc(s_wr_t, 1)
            dve.wait_ge(s_std, 1)
            link(dve.reciprocal(rstd[:, :], ln_tmp[:, :]))
            link(dve.tensor_tensor(ln_tmp[:, :], rstd[:, :], rstd[:, :], ALU.mult))
            link(dve.tensor_tensor(ln_tmp[:, :], ln_tmp[:, :], var[:, :], ALU.mult))
            link(dve.tensor_scalar(ln_tmp[:, :], ln_tmp[:, :], -0.5, 1.5, ALU.mult, ALU.add))
            link(dve.tensor_tensor(rstd[:, :], rstd[:, :], ln_tmp[:, :], ALU.mult))
            def normed(j):
                for u in range(NX):
                    b = NX * j + u
                    wait(dve, s_xn_ps, NX * j)
                    wait(dve, s_xst[u], 16 * j)
                    dve.tensor_scalar(xn[:, u, :], xa[:, bass.ds(b, 1), :].rearrange("p b d -> p (b d)"), mean[:, bass.ds(b, 1)],
                                      rstd[:, bass.ds(b, 1)], ALU.subtract, ALU.mult).then_inc(s_xn, 1)

            looped(dve, B // NX, normed)

            dve.wait_ge(s_iota, 3)
            dve.tensor_copy(iota_c[:, :], iota_ci[:, :])
            dve.tensor_copy(iota_p[:, :], iota_pi[:, :])
            link(dve.tensor_copy(value[:, :, :], value_i[:, :, :]))
            dve.tensor_scalar(first_e[:, :], iota_c[0:SQ, 0:NE], -1.0, float(NE), ALU.mult, ALU.add)
            link(dve.tensor_scalar(thresh[:, :], iota_c[0:SQ, 0:PER_E], float(P), None, ALU.mult))

            bne = [SQ, B, NE]
            logits = ps[0:SQ, LOGIT, 0:B * NE].rearrange("p (b e) -> p b e", e=NE)
            dve.wait_ge(s_logit, B)
            link(dve.tensor_reduce(col[:, :], logits, axis=AX.X, op=ALU.max))
            dve.tensor_tensor(tmp[:, :, :], logits, bcast(col[:, :], bne, 2), ALU.subtract).then_inc(s_shift, 1)
            dve.wait_ge(s_exp, 1)
            link(dve.tensor_reduce(col[:, :], probs[:, :, :], axis=AX.X, op=ALU.add))
            link(dve.reciprocal(col[:, :], col[:, :]))
            link(dve.tensor_tensor(probs[:, :, :], probs[:, :, :], bcast(col[:, :], bne, 2), ALU.mult))
            for k, mask in enumerate((mask1, mask2)):
                link(dve.tensor_reduce(gates[:, k, :], probs[:, :, :], axis=AX.X, op=ALU.max))
                link(dve.tensor_tensor(tmp[:, :, :], probs[:, :, :], bcast(gates[:, k, :], bne, 2), ALU.is_equal))
                link(dve.tensor_tensor(tmp[:, :, :], tmp[:, :, :], bcast(first_e[:, :], bne, 1), ALU.mult))
                link(dve.tensor_reduce(col[:, :], tmp[:, :, :], axis=AX.X, op=ALU.max))
                link(dve.tensor_tensor(mask[:, :, :], tmp[:, :, :], bcast(col[:, :], bne, 2), ALU.is_equal))
                if k == 0:
                    link(dve.scalar_tensor_tensor(out=probs[:, :, :], in0=mask[:, :, :], scalar=-2.0, in1=probs[:, :, :],
                                                  op0=ALU.mult, op1=ALU.add))
            dve.tensor_tensor(both[:, :, :], mask1[:, :, :], mask2[:, :, :], ALU.add).then_inc(s_both, 1)
            dve.wait_ge(s_tanh, 1)
            link(dve.tensor_scalar(gates[:, :, :], gates[:, :, :], tanh_f[:, :], None, ALU.mult))

            dve.wait_ge(s_rank, 1)
            rank = ps[0:SQ, RANK, :].rearrange("p (h b e) -> p h b e", h=2, e=NE)
            dve.tensor_copy(cum_a[:, :, :], rank[:, 1, :, :])
            link(dve.tensor_copy(totals[:, :, :], rank[:, 1, :, :]))
            old, new, d = cum_a, cum_b, 1
            while d < B:
                dve.tensor_copy(new[:, 0:d, :], old[:, 0:d, :])
                link(dve.tensor_tensor(new[:, d:B, :], old[:, d:B, :], old[:, 0:B - d, :], ALU.add))
                old, new, d = new, old, 2 * d
            counts = old[:, B - 1, :]
            link(dve.tensor_tensor(cmp[:, :, :], bcast(counts, [SQ, NE, PER_E], 2), bcast(thresh[:, :], [SQ, NE, PER_E], 1), ALU.is_gt))
            link(dve.tensor_reduce(n_tiles[:, :], cmp[:, :, :], axis=AX.X, op=ALU.add))
            link(dve.tensor_copy(ct_a[:, :], n_tiles[:, :]))
            co, cn, d = ct_a, ct_b, 1
            while d < NE:
                dve.tensor_copy(cn[:, 0:d], co[:, 0:d])
                link(dve.tensor_tensor(cn[:, d:NE], co[:, d:NE], co[:, 0:NE - d], ALU.add))
                co, cn, d = cn, co, 2 * d
            link(dve.tensor_tensor(base[:, :], co[:, :], n_tiles[:, :], ALU.subtract))
            link(dve.tensor_scalar(base[:, :], base[:, :], float(P), None, ALU.mult))
            link(dve.tensor_tensor(slot_e[:, :, :], old[:, :, :], totals[:, :, :], ALU.subtract))
            link(dve.tensor_tensor(slot_e[:, :, :], slot_e[:, :, :], rank[:, 0, :, :], ALU.add))
            link(dve.tensor_tensor(slot_e[:, :, :], slot_e[:, :, :], bcast(base[:, :], bne, 1), ALU.add))
            for k, mask in enumerate((mask1, mask2)):
                link(dve.tensor_tensor(tmp[:, :, :], mask[:, :, :], slot_e[:, :, :], ALU.mult))
                link(dve.tensor_reduce(slots[:, k, :], tmp[:, :, :], axis=AX.X, op=ALU.add))
            link(dve.tensor_scalar(tile_no[:, :, :], slots[:, :, :], 1.0 / P, -(P - 1) / (2.0 * P), ALU.mult, ALU.add))
            link(dve.tensor_scalar(tile_no[:, :, :], tile_no[:, :, :], MAGIC, None, ALU.add))
            link(dve.tensor_scalar(tile_no[:, :, :], tile_no[:, :, :], -MAGIC, None, ALU.add))
            link(dve.scalar_tensor_tensor(out=row_no[:, :, :], in0=tile_no[:, :, :], scalar=-float(P), in1=slots[:, :, :],
                                          op0=ALU.mult, op1=ALU.add))
            def placed(j):
                for k in range(TOP):
                    wait(dve, s_table, TOP * j)
                    dve.tensor_scalar(one_row[:, k, :], iota_c[0:SQ, :], row_no[:, k, bass.ds(j, 1)], None, ALU.is_equal)
                    dve.tensor_scalar(one_val[:, k, 0, :], iota_c[0:SQ, 0:TW], tile_no[:, k, bass.ds(j, 1)], value[:, k, bass.ds(j, 1)],
                                      ALU.is_equal, ALU.mult)
                    dve.tensor_scalar(one_val[:, k, 1, :], iota_c[0:SQ, 0:TW], tile_no[:, k, bass.ds(j, 1)], gates[:, k, bass.ds(j, 1)],
                                      ALU.is_equal, ALU.mult).then_inc(s_onehot, 1)

            looped(dve, B, placed)
            link(dve.tensor_tensor(e_cmp[:, :, :], bcast(co[0:1, :], [1, TW, NE], 1), bcast(iota_c[0:1, 0:TW], [1, TW, NE], 2), ALU.is_le))
            link(dve.tensor_reduce(e_tile[:, :], e_cmp[:, :, :], axis=AX.X, op=ALU.add))
            link(dve.tensor_scalar(e_tile[:, :], e_tile[:, :], float(NE - 1), None, ALU.min))
            link(dve.tensor_copy(e_idx[:, :], e_tile[:, :]))
            dve.wait_ge(s_table, TOP * B + 1)
            table = ps[:, TABLE, 0:2 * TW].rearrange("p (h t) -> p h t", h=2)
            link(dve.tensor_copy(gate_s[:, :], table[:, 1, :]))
            link(dve.tensor_scalar(t_pad[:, :], table[:, 0, :], 0.0, None, ALU.is_equal))
            link(dve.tensor_tensor(t_pad[:, :], t_pad[:, :], iota_p[:, :], ALU.mult))
            link(dve.scalar_tensor_tensor(out=t_dst[:, :], in0=table[:, 0, :], scalar=float(TOP * TOK), in1=t_pad[:, :], op0=ALU.add, op1=ALU.add))
            link(dve.tensor_copy(dst_idx[:, :], t_dst[:, :]))
            link(dve.tensor_scalar(t_src[:, :], t_dst[:, :], 0.5, -0.25, ALU.mult, ALU.add))
            link(dve.tensor_scalar(t_src[:, :], t_src[:, :], MAGIC, None, ALU.add))
            link(dve.tensor_scalar(t_src[:, :], t_src[:, :], -MAGIC, float(TOK - 1), ALU.add, ALU.min))
            dve.tensor_copy(src_idx[:, :], t_src[:, :]).then_inc(s_tables, 1)
            dve.wait_ge(s_tables, 1)

            def step(o, m, x, g):
                if g:
                    wait(dve, s_xg[g[1]], 16 * g[0])
                    dve.tensor_copy(idx_g[:, g[1], :], src_idx[:, bass.ds(num(g), 1)]).then_inc(s_idx, 1)
                if o:
                    wait(dve, s_y_ps, num(o) + 1)
                    wait(dve, s_yout[o[1]], 16 * o[0])
                    dve.tensor_copy(idx_y[:, o[1], :], dst_idx[:, bass.ds(num(o), 1)])
                    dve.tensor_scalar(y[:, o[1], :], ps[:, YB, 0:EMB], gate_s[:, bass.ds(num(o), 1)], None, ALU.mult).then_inc(s_y, 1)
                if m:
                    wait(dve, s_silu, num(m) + 1)
                    wait(dve, s_b, num(m) + 1)
                    wait(dve, s_h_ps, num(m))
                    dve.tensor_tensor(h[:, 0:F], silu[:, :], ps[:, BB, 0:F], ALU.mult).then_inc(s_h, 1)

            pipeline(dve, step)
            for g in range(B // 4):
                dve.wait_ge(s_yk[g % 2], 16 * (g // 2 + 1))
                rows = xa[:, 4 * g:4 * g + 4, :]
                dve.tensor_tensor(rows, rows, yk[:, g % 2, :, 0:EMB], ALU.add).then_inc(s_res, 1)
                dve.wait_ge(s_res, g + 1)
                dve.tensor_tensor(rows, rows, yk[:, g % 2, :, EMB:2 * EMB], ALU.add).then_inc(s_add, 1)

        @block.tensor
        def _(pe):
            pe.wait_ge(s_wr, 32)
            for k in range(DC):
                last = pe.transpose(ps[:, 0, NE * k:NE * k + NE], wr_sb[:, P * k:P * k + P], ident[0:NE, 0:NE])
            last.then_inc(s_wr_ps, 1)
            pe.wait_ge(s_wr_t, 1)
            def logits_of(j):
                for u in range(NX):
                    wait(pe, s_xn, NX * j + u + 1)
                    wait(pe, s_xn_t, NX * j)
                    for m in range(DC):
                        last = pe.transpose(ps[:, u, SQ * m:SQ * m + SQ], xn[:, u, P * m:P * m + P], ident[0:SQ, 0:SQ])
                    last.then_inc(s_xn_ps, 1)
                for u in range(NX):
                    wait(pe, s_xn_t, NX * j + u + 1)
                    logit = ps[0:SQ, LOGIT, 0:B * NE].rearrange("p (j n) -> p j n", n=NX * NE)[:, bass.ds(j, 1), NE * u:NE * u + NE]
                    for m in range(DC):
                        last = pe.matmul(logit.rearrange("p j n -> p (j n)"), xn_t[:, u, m, :], wr_t[:, m, :], start=(m == 0), stop=(m == DC - 1))
                    last.then_inc(s_logit, 1)

            looped(pe, B // NX, logits_of)
            pe.wait_ge(s_both, 1)
            pe.wait_ge(s_shape, 5)
            pe.matmul(ps[0:SQ, RANK, 0:B * NE], before[:, :], both[:, :, :].rearrange("p b e -> p (b e)"), start=True, stop=True)
            pe.matmul(ps[0:SQ, RANK, B * NE:2 * B * NE], ones[:, :], both[:, :, :].rearrange("p b e -> p (b e)"), start=True, stop=True).then_inc(s_rank, 1)
            pe.matmul(ps[:, TABLE, 0:2 * TW], zeros[:, :], zeros[:, :], start=True, stop=False)
            def counted_in(j):
                for k in range(TOP):
                    wait(pe, s_onehot, TOP * j + k + 1)
                    pe.matmul(ps[:, TABLE, 0:2 * TW], one_row[:, k, :], one_val[:, k, :, :].rearrange("p h t -> p (h t)"),
                              start=False, stop=False).then_inc(s_table, 1)

            looped(pe, B, counted_in)
            pe.matmul(ps[:, TABLE, 0:2 * TW], zeros[:, :], zeros[:, :], start=False, stop=True).then_inc(s_table, 1)
            pe.wait_ge(s_tables, 1)
            pe.wait_ge(s_w, 16 * (2 * DC + FC))

            def expert(t):
                return pe.value_load(e_idx[0:1, bass.ds(num(t), 1)], min_val=0, max_val=NE - 1)

            def inner(t, w, bank, e, s):
                for k in range(DC):
                    last = pe.matmul(ps[:, bank, 0:F], xg_t[:, t[1], k, :], w[:, k, bass.ds(e, 1), :].rearrange("p e f -> p (e f)"),
                                     start=(k == 0), stop=(k == DC - 1))
                last.then_inc(s, 1)

            def step(o, m, x, g):
                if m:
                    e_m = expert(m)
                    wait(pe, s_xg_t, num(m) + 1)
                    wait(pe, s_silu, num(m))
                    inner(m, w1_sb, AB, e_m, s_a)
                if o:
                    wait(pe, s_h, num(o) + 1)
                    wait(pe, s_h_t, num(o))
                    for c in range(FC):
                        last = pe.transpose(ps[:, HTB, P * c:P * c + P], h[:, P * c:P * c + P], ident[:, :])
                    last.then_inc(s_h_ps, 1)
                if x:
                    wait(pe, s_xg[x[1]], 16 * (x[0] + 1))
                    wait(pe, s_xg_t, num(x))
                    for k in range(DC):
                        last = pe.transpose(ps[:, XTB, P * k:P * k + P], xg[:, x[1], P * k:P * k + P], ident[:, :])
                    last.then_inc(s_xg_ps, 1)
                if m:
                    wait(pe, s_h, num(m))
                    inner(m, w3_sb, BB, e_m, s_b)
                if o:
                    e_o = expert(o)
                    wait(pe, s_h_t, num(o) + 1)
                    wait(pe, s_y, num(o))
                    for c in range(FC):
                        n = min(P, F - P * c)
                        last = pe.matmul(ps[:, YB, 0:EMB], h_t[0:n, c, :], w2_sb[0:n, c, bass.ds(e_o, 1), :].rearrange("p e d -> p (e d)"),
                                         start=(c == 0), stop=(c == FC - 1))
                    last.then_inc(s_y_ps, 1)

            pipeline(pe, step)


_INS = ['x', 'ctx_1024', 'g_xattn', 'g_ffn', 'L0_xattn_Wq', 'L0_xattn_bq', 'L0_xattn_Wk', 'L0_xattn_bk', 'L0_xattn_Wv',
        'L0_xattn_bv', 'L0_xattn_Wo', 'L0_xattn_bo', 'L0_ffn_w_router', 'L0_ffn_w1', 'L0_ffn_w2', 'L0_ffn_w3']


def kernel(**inputs):
    import numpy as np
    import concourse.bacc as bacc
    from concourse.bass_utils import run_bass_kernel_spmd

    nc = bacc.Bacc("TRN2", target_bir_lowering=False, num_devices=1)
    arrays, args = {}, []
    for name in _INS:
        a = np.ascontiguousarray(inputs[name])
        arrays[f"in_{name}_dram"] = a
        args.append(nc.dram_tensor(f"in_{name}_dram", a.shape, mybir.dt.from_np(a.dtype), kind="ExternalInput").ap())
    args.append(nc.dram_tensor("out_0_dram", inputs['x'].shape, mybir.dt.float32, kind="ExternalOutput").ap())
    flamingo(nc, *args)
    r = run_bass_kernel_spmd(nc, [arrays], core_ids=[0])
    return r.results[0]["out_0_dram"]
```
